# Optimizing a Trainium2 kernel written in Bass

```python
import numpy as np
import jax
import jax.numpy as jnp

def _softmax(x, axis=-1):
    return jax.nn.softmax(x, axis=axis)

def _gelu(x):
    return jax.nn.gelu(x, approximate=True)

def _silu(x):
    return jax.nn.silu(x)

def _sigmoid(x):
    return jax.nn.sigmoid(x)

def _layernorm(x, axis=-1, eps=1e-05):
    m = jnp.mean(x, axis=axis, keepdims=True)
    v = jnp.var(x, axis=axis, keepdims=True)
    return (x - m) / jnp.sqrt(v + eps)

def _scatter_add(tgt, idx, src, axis=0):
    return tgt.at[idx].add(src)

def _segment_sum(src, seg, n):
    return jax.ops.segment_sum(src, seg, n)
kernel_name = 'mk_rec_standalone_d1_rec_r8_61f274'

def setup_inputs(seed: int=0):
    np.random.seed(seed)
    _w = jnp.asarray

    def _rec_inputs():
        import jax
        import jax.numpy as jnp
        _rk = jax.random.key(seed)
        r_x_emb = -0.000849101 + 1.0004 * jax.random.normal(jax.random.fold_in(_rk, 1), (512, 39, 16), jnp.float32)
        return r_x_emb
    r_x_emb = _rec_inputs()

    def _L0_rec_setup():
        import jax, jax.numpy as jnp
        import numpy as np
        NUM_FIELD = 39
        CIN_SIZE = [128, 128]
        EMBED_DIM = 16
        BATCH = 256
        key = jax.random.key(seed)
        k1, k2, k3 = jax.random.split(key, 3)
        x_emb = jax.random.normal(k1, (BATCH, NUM_FIELD, EMBED_DIM), dtype=jnp.float32)
        W0 = jax.random.normal(k2, (CIN_SIZE[0], NUM_FIELD * NUM_FIELD), dtype=jnp.float32) * 0.02
        W1 = jax.random.normal(k3, (CIN_SIZE[1], CIN_SIZE[0] * NUM_FIELD), dtype=jnp.float32) * 0.02
        return {'x_emb': x_emb, 'W0': W0, 'W1': W1}
    _L0_rec_all = _L0_rec_setup()
    _L0_rec_in = {k: v for k, v in _L0_rec_all.items() if k in ('W0', 'W1')}
    del _L0_rec_all
    return {'r_x_emb': r_x_emb, 'L0_rec_W0': _L0_rec_in['W0'], 'L0_rec_W1': _L0_rec_in['W1']}

def reference(r_x_emb, L0_rec_W0, L0_rec_W1):
    import jax
    import jax.numpy as jnp

    def _L0_rec_ref(x_emb, W0, W1):
        import jax, jax.numpy as jnp
        import numpy as np
        NUM_FIELD = 39
        CIN_SIZE = [128, 128]
        EMBED_DIM = 16
        BATCH = 256
        B, F, D = x_emb.shape
        x = x_emb
        outs = []
        for W in (W0, W1):
            last = x.shape[1]
            inter = (x[:, :, None, :] * x_emb[:, None, :, :]).reshape(B, last * F, D)
            x = jnp.einsum('bid,hi->bhd', inter, W)
            outs.append(x.sum(axis=-1))
        return jnp.concatenate(outs, axis=-1)
    y = _L0_rec_ref(r_x_emb, L0_rec_W0, L0_rec_W1)
    return y

_drawn_inputs = setup_inputs


def setup_inputs(seed=0):
    import zlib

    import numpy as np

    out = dict(_drawn_inputs(seed))
    spreads = {}
    factors = {}
    for name, (base, spread) in spreads.items():
        noise = np.random.default_rng([zlib.crc32(name.encode()), seed]).standard_normal(out[name].shape)
        drawn = base * np.exp(spread * noise) if base else spread * noise
        out[name] = jnp.asarray(drawn.astype(out[name].dtype))
    for name, factor in factors.items():
        out[name] = (out[name] * factor).astype(out[name].dtype)
    return out
```

```python
from contextlib import ExitStack

import concourse.bass as bass
import numpy as np
from concourse import mybir

F32 = mybir.dt.float32
F32R = mybir.dt.float32r
ALU = mybir.AluOpType
ACT = mybir.ActivationFunctionType

P = 128
B = 512
F = 39
D = 16
H = 128
COLS = B * D
CW = 512
CHUNKS = COLS // CW
GROUP = P // D
GROUPS = CW // P
FO = F + 1
GW = GROUP * FO
FULL = 6
TILES = FULL + 1
STEPS = TILES // 2 + 1
HALF = B // 2
PARTS = 3
PJ = F // PARTS

ROW_FIELD = (list(range(F)) + list(range(64 - F)) + list(range(F)) + list(range(64 - F, F)))
ROW_FIELD += list(range(P - len(ROW_FIELD)))
SQUARE_ROWS = (0, 32, 64, 96)


def plan_pairs():
    room = {i: FULL * ROW_FIELD.count(i) for i in range(F)}
    owned = {i: [] for i in range(F)}

    def place(pair, seen):
        for i in sorted(set(pair), key=lambda i: len(owned[i]) - room[i]):
            if i in seen:
                continue
            seen.add(i)
            if len(owned[i]) < room[i]:
                owned[i].append(pair)
                return True
            for other in list(owned[i]):
                if other[0] != other[1] and place(other, seen):
                    owned[i].remove(other)
                    owned[i].append(pair)
                    return True
        return False

    for i in range(F):
        for j in range(i + 1, F):
            assert place((i, j), set())
    squares = [i for i in range(F) if not place((i, i), set())]
    assert len(squares) == F * (F + 1) // 2 - FULL * P
    pairs = []
    for i in ROW_FIELD:
        pairs.append([(i, sum(pair) - i) for pair in (owned[i].pop() for _ in range(FULL))])
    return pairs, squares


def build(nc, x_rows, x_groups, placing, identity, owner, w0_ij, w0_ji, w1, out):
    ctx = ExitStack()
    with ctx:
        def sb(name, shape, dt=F32):
            return ctx.enter_context(nc.sbuf_tensor(name, shape, dt))

        def ps(name, shape):
            return ctx.enter_context(nc.psum_tensor(name, shape, F32))

        def sem(name):
            return ctx.enter_context(nc.semaphore(name))

        stage = sb("stage", [P, 2 * TILES * H])
        w0_high = sb("w0_high", [P, TILES, H], F32R)
        w0_low = sb("w0_low", [P, FULL, H], F32R)
        w1_high = sb("w1_high", [P, F, H], F32R)
        w1_low = sb("w1_low", [P, F, H], F32R)
        place = sb("place", [P, TILES, P], F32R)
        ident = sb("ident", [P, P])
        ones8 = sb("ones8", [P, GROUP])
        x_in = sb("x_in", [P, 4 * CW])
        x_split = sb("x_split", [P, 2, CW], F32R)
        z = sb("z", [P, 2, 2 * CW])
        squares = sb("squares", [P, CW])
        z_high = sb("z_high", [P, TILES, CW], F32R)
        z_low = sb("z_low", [P, FULL, CW], F32R)
        x1 = sb("x1", [P, CW])
        x1t_high = sb("x1t_high", [P, CW], F32R)
        x1t_low = sb("x1t_low", [P, CW], F32R)
        xg_in = sb("xg_in", [P, 2, GROUPS, F])
        xg = sb("xg", [P, 2, 2, 2, 2, F], F32R)
        blocks = sb("blocks", [P, 2, 2, 2, GW], F32R)
        p_high = sb("p_high", [P, FO, HALF], F32R)
        p_low = sb("p_low", [P, FO, HALF], F32R)
        sums = sb("sums", [P, 2, HALF])

        placed = [ps(f"placed{k}", [P, 2 * CW]) for k in range(2)]
        x1_acc = [ps(f"x1_acc{k}", [P, CW]) for k in range(2)]
        turned = ps("turned", [P, CW])
        p_acc = ps("p_acc", [P, CW])
        out_acc = p_acc[:, 0:HALF]

        constants_in = [sem(f"constants_in{k}") for k in range(3)]
        weights_in = sem("weights_in")
        weights_high = sem("weights_high")
        weights_low = sem("weights_low")
        w0_summed = sem("w0_summed")
        place_ready = sem("place_ready")
        blocks_zero = sem("blocks_zero")
        blocks_ones = sem("blocks_ones")
        x_loaded = [sem(f"x_loaded{k}") for k in range(2)]
        xg_loaded = [sem(f"xg_loaded{k}") for k in range(2)]
        x_high_done = sem("x_high_done")
        x_low_done = sem("x_low_done")
        xg_high_done = sem("xg_high_done")
        xg_low_done = sem("xg_low_done")
        blocks_loaded = [sem(f"blocks_loaded{q}") for q in range(2)]
        placed_done = sem("placed_done")
        z_done = sem("z_done")
        squares_done = sem("squares_done")
        high_done = sem("high_done")
        low_a_done = sem("low_a_done")
        low_b_done = sem("low_b_done")
        step_done = sem("step_done")
        x1_out = sem("x1_out")
        x1_turned = sem("x1_turned")
        turned_high = sem("turned_high")
        turned_low = sem("turned_low")
        p_done = sem("p_done")
        p_high_done = sem("p_high_done")
        p_low_done = sem("p_low_done")
        out_done = sem("out_done")
        out_copied = sem("out_copied")
        x1_sums = sem("x1_sums")
        stored = sem("stored")

        W0_DONE = 3
        W1_DONE = W0_DONE + PARTS
        MIDDLE, END = CHUNKS // 4, CHUNKS // 2 - 1
        block = ctx.enter_context(nc.Block())

        def slot(c):
            return bass.ds((c % 4) * CW, CW)

        def batch(c, g):
            return bass.ds((c % (CHUNKS // 2)) * (GROUPS * GROUP) + g * GROUP, GROUP)

        def seen(m, k):
            return min(2 * m + k, 2) if isinstance(m, int) else 2

        def middle(m, k):
            return isinstance(m, int) and (m, k) == (MIDDLE, 1)

        def last_two(m, k):
            last = ((m, 0) if k == 1 else (m - 1, 1)) if seen(m, k) >= 1 else None
            return last, (m - 1, k) if seen(m, k) >= 2 else None

        last_acc = [a[:, 0:GW] for a in (p_acc, placed[0], placed[1])] + [placed[0][:, CW:CW + GW]]

        @block.sync
        def _(sp):
            def load_x(c, k):
                sp.dma_start(x_in[:, slot(c)], x_rows[:, bass.ds(c * CW, CW)]).then_inc(x_loaded[k], 16)

            def load_xg(c, k):
                sp.dma_start(xg_in[:, k], x_groups[:, bass.ds(c * GROUPS, GROUPS), :])\
                    .then_inc(xg_loaded[k], 16)

            def load_w1(part):
                sp.wait_ge(weights_low, W0_DONE + part)
                sp.dma_start(stage[:, 0:PJ * H], w1[:, part * PJ:(part + 1) * PJ, :])\
                    .then_inc(weights_in, 16)

            def chunk(m, k, load_ahead=True, load_g=True):
                c = 2 * m + k
                if load_ahead:
                    to, at = ((c + 4) % 4 * CW, (c + 4) * CW)
                    if not isinstance(m, int):
                        to, at = sp.snap(to), sp.snap(at)
                    sp.wait_ge(x_low_done, c + 1)
                    sp.wait_ge(z_done, 3 * c + 3)
                    sp.wait_ge(x_loaded[k], 16 * (m + 2))
                    sp.dma_start(x_in[:, bass.ds(to, CW)], x_rows[:, bass.ds(at, CW)]).then_inc(x_loaded[k], 16)
                sp.wait_ge(xg_high_done, c + 1)
                sp.wait_ge(xg_low_done, c + 1)
                if load_g:
                    load_xg(c + 2, k)
                if seen(m, k) == 0:
                    sp.wait_ge(blocks_ones, 4)
                for q in range(2):
                    if seen(m, k) >= 1:
                        sp.wait_ge(p_done, GROUPS * (c - 1) + 2 * q + 2)
                    for b in range(GROUP):
                        rows = slice(D * b, D * b + D)
                        sp.dma_start(blocks[rows, q, :, :, FO * b:FO * b + F].bitcast(F32),
                                     xg[rows, k, q].bitcast(F32)).then_inc(blocks_loaded[q], 16)

            def store(h):
                sp.wait_ge(x1_sums, h + 1)
                sp.dma_start(out[0:H, h * HALF:(h + 1) * HALF], sums[:, 0, :]).then_inc(stored, 16)
                sp.wait_ge(out_copied, h + 1)
                sp.dma_start(out[H:2 * H, h * HALF:(h + 1) * HALF], sums[:, 1, :]).then_inc(stored, 16)

            sp.dma_start(z[:, 1, 0:TILES * P], placing[:, :]).then_inc(constants_in[0], 16)
            load_x(0, 0)
            load_x(1, 1)
            sp.dma_start(stage[:, 0:TILES * H], w0_ij[:, :]).then_inc(weights_in, 16)
            sp.dma_start(stage[:, TILES * H:], w0_ji[:, :]).then_inc(weights_in, 16)
            sp.dma_start(ident[:, :], identity[:, :]).then_inc(constants_in[1], 16)
            sp.dma_start(ones8[:, :], owner[:, :]).then_inc(constants_in[2], 16)
            for k in range(2):
                load_xg(k, k)
            for k in range(2):
                sp.wait_ge(x_loaded[k], 16)
                load_x(2 + k, k)
            load_w1(0)
            chunk(0, 0)
            load_w1(1)
            chunk(0, 1)
            load_w1(2)
            with sp.Fori(1, MIDDLE) as m:
                chunk(m, 0)
                chunk(m, 1)
            chunk(MIDDLE, 0)
            chunk(MIDDLE, 1)
            store(0)
            chunk(END - 2, 0)
            chunk(END - 2, 1)
            chunk(END - 1, 0, load_ahead=False)
            chunk(END - 1, 1, load_ahead=False)
            chunk(END, 0, load_ahead=False, load_g=False)
            chunk(END, 1, load_ahead=False, load_g=False)
            store(1)
            sp.wait_ge(stored, 4 * 16)

        @block.gpsimd
        def _(pool):
            def split_x(m, k):
                pool.wait_ge(x_high_done, 2 * m + k + 1)
                lower = x_split[64:P, k, :]
                pool.tensor_tensor(lower, x_in[64:P, slot(2 * m + k)], lower.bitcast(F32), ALU.subtract)\
                    .then_inc(x_low_done, 1)

            def split_xg(m, k):
                c = 2 * m + k
                pool.wait_ge(xg_high_done, c + 1)
                if seen(m, k) >= 2:
                    for q in range(2):
                        pool.wait_ge(blocks_loaded[q], 16 * GROUP * (c - 1))
                pool.tensor_tensor(xg[:, k, :, 1], xg_in[:, k].rearrange("p (q g) j -> p q g j", q=2),
                                   xg[:, k, :, 0].bitcast(F32), ALU.subtract)\
                    .then_inc(xg_low_done, 1)

            def chunk(m, k, split_next=True):
                c = 2 * m + k
                if seen(m, k) >= 1:
                    pool.wait_ge(low_b_done, STEPS * c)
                pool.wait_ge(x_low_done, min(c + 2, CHUNKS) if isinstance(c, int) else c + 2)
                split_xg(m, k)
                for s in range(STEPS - 1):
                    pool.wait_ge(high_done, STEPS * c + s + 1)
                    if seen(m, k) >= 1:
                        pool.wait_ge(step_done, STEPS * (c - 1) + s + 1)
                    pool.tensor_tensor(z_low[:, 2 * s + 1, :], z[:, (k + s) % 2, CW:2 * CW],
                                       z_high[:, 2 * s + 1, :].bitcast(F32), ALU.subtract)\
                        .then_inc(low_b_done, 1)
                pool.wait_ge(high_done, STEPS * c + STEPS)
                pool.wait_ge(low_b_done, STEPS * c + STEPS - 1)
                lower = z_high[64:P, TILES - 1, :]
                pool.tensor_tensor(lower, squares[64:P, :], lower.bitcast(F32), ALU.subtract)\
                    .then_inc(low_b_done, 1)
                if split_next:
                    split_x(m + 1, k)

            pool.memset(blocks[:, :, :, :, :].bitcast(F32), 0.0).then_inc(blocks_zero, 1)
            pool.wait_ge(blocks_zero, 1)
            split_x(0, 0)
            split_x(0, 1)
            chunk(0, 0)
            chunk(0, 1)
            with pool.Fori(1, END) as m:
                chunk(m, 0)
                chunk(m, 1)
            chunk(END, 0, split_next=False)
            chunk(END, 1, split_next=False)

        @block.scalar
        def _(act):
            def split_x(m, k):
                c = 2 * m + k
                act.wait_ge(x_loaded[k], 16 * (m + 1))
                if seen(m, k) >= 2:
                    act.wait_ge(placed_done, STEPS * (c - 1))
                act.activation(x_split[:, k, :], x_in[:, slot(c)], ACT.Copy).then_inc(x_high_done, 1)

            def split_xg(m, k):
                c = 2 * m + k
                act.wait_ge(xg_loaded[k], 16 * (m + 1))
                if seen(m, k) >= 2:
                    for q in range(2):
                        act.wait_ge(blocks_loaded[q], 16 * GROUP * (c - 1))
                act.activation(xg[:, k, :, 0], xg_in[:, k].rearrange("p (q g) j -> p q g j", q=2), ACT.Copy)\
                    .then_inc(xg_high_done, 1)

            def high(m, k, s):
                c = 2 * m + k
                act.wait_ge(z_done, 3 * c + s + 1)
                if seen(m, k) >= 1:
                    act.wait_ge(step_done, STEPS * (c - 1) + s + 1)
                act.activation(z_high[:, 2 * s:2 * s + 2, :], z[:, (k + s) % 2, :], ACT.Copy)\
                    .then_inc(high_done, 1)

            def square(m, k):
                c = 2 * m + k
                act.wait_ge(placed_done, STEPS * (c + 1))
                if seen(m, k) >= 1:
                    act.wait_ge(step_done, STEPS * c)
                    act.wait_ge(low_b_done, STEPS * c)
                act.activation(squares[64:P, :], placed[1][64:P, 0:CW], ACT.Square).then_inc(squares_done, 1)
                act.wait_ge(squares_done, c + 1)
                act.activation(z_high[:, TILES - 1, :], placed[1][:, 0:CW], ACT.Square).then_inc(high_done, 1)

            def x1_to_sbuf(m, k):
                c = 2 * m + k
                act.wait_ge(step_done, STEPS * (c + 1))
                if seen(m, k) >= 1:
                    act.wait_ge(x1_turned, c)
                act.activation(x1[:, :], x1_acc[k][:, :], ACT.Copy).then_inc(x1_out, 1)

            def turned_to_high(m, k):
                c = 2 * m + k
                act.wait_ge(x1_turned, c + 1)
                if seen(m, k) >= 1:
                    act.wait_ge(p_done, GROUPS * c)
                act.activation(x1t_high[:, :], turned[:, :], ACT.Copy).then_inc(turned_high, 1)

            def p_to_high(m, k, g, acc=p_acc[:, 0:GW]):
                c = 2 * m + k
                act.wait_ge(p_done, GROUPS * c + g + 1)
                act.activation(p_high[:, :, batch(c, g)], acc.rearrange("p (b j) -> p j b", b=GROUP),
                               ACT.Copy).then_inc(p_high_done, 1)

            def split_w1(part):
                act.wait_ge(weights_in, 16 * (3 + part))
                act.activation(w1_high[:, part * PJ:(part + 1) * PJ, :], stage[:, 0:PJ * H], ACT.Copy)\
                    .then_inc(weights_high, 1)

            def out_to_sbuf(h):
                act.wait_ge(out_done, h + 1)
                if h >= 1:
                    act.wait_ge(stored, 2 * 16 * h)
                act.activation(sums[:, 1, :], out_acc, ACT.Copy).then_inc(out_copied, 1)

            def chunk(m, k, split_next=True):
                last, before = last_two(m, k)
                split_xg(m, k)
                high(m, k, 0)
                if before:
                    p_to_high(*before, 1)
                high(m, k, 1)
                if before:
                    p_to_high(*before, 2)
                if last:
                    x1_to_sbuf(*last)
                high(m, k, 2)
                if before:
                    p_to_high(*before, 3)
                if last:
                    turned_to_high(*last)
                square(m, k)
                if split_next:
                    split_x(m + 1, k)
                if middle(m, k):
                    out_to_sbuf(0)
                    act.wait_ge(x1_sums, 1)
                if last:
                    p_to_high(*last, 0)

            act.wait_ge(constants_in[0], 16)
            act.activation(place[:, :, :], z[:, 1, 0:TILES * P], ACT.Copy).then_inc(place_ready, 1)
            split_x(0, 0)
            split_x(0, 1)
            act.wait_ge(w0_summed, 1)
            act.activation(w0_high[:, :, :], stage[:, 0:TILES * H], ACT.Copy).then_inc(weights_high, 1)
            act.wait_ge(constants_in[2], 16)
            act.wait_ge(blocks_zero, 1)
            for q in range(2):
                for g in range(2):
                    act.activation(blocks[:, q, 0, g, F::FO], ones8[:, :], ACT.Copy).then_inc(blocks_ones, 1)
            chunk(0, 0)
            split_w1(0)
            chunk(0, 1)
            split_w1(1)
            with act.Fori(1, MIDDLE) as m:
                chunk(m, 0)
                chunk(m, 1)
            split_w1(2)
            chunk(MIDDLE, 0)
            chunk(MIDDLE, 1)
            with act.Fori(MIDDLE + 1, END) as m:
                chunk(m, 0)
                chunk(m, 1)
            chunk(END, 0, split_next=False)
            chunk(END, 1, split_next=False)
            for g in range(1, GROUPS):
                p_to_high(END, 0, g)
            x1_to_sbuf(END, 1)
            turned_to_high(END, 1)
            for g in range(GROUPS):
                p_to_high(END, 1, g, acc=last_acc[g])
            out_to_sbuf(1)

        @block.vector
        def _(dve):
            def product(m, k, s):
                c = 2 * m + k
                dve.wait_ge(placed_done, STEPS * c + s + 1)
                if s == 2:
                    dve.wait_ge(low_a_done, 3 * c + 1)
                    dve.wait_ge(low_b_done, STEPS * c + 1)
                elif seen(m, k) >= 1:
                    dve.wait_ge(low_a_done, 3 * (c - 1) + s + 2)
                    dve.wait_ge(low_b_done, STEPS * (c - 1) + s + 2)
                dve.tensor_tensor(z[:, (k + s) % 2, :].rearrange("p (t n) -> p t n", t=2),
                                  placed[s % 2][:, :].rearrange("p (t n) -> p t n", t=2),
                                  x_in[:, slot(c)].unsqueeze(1).to_broadcast([P, 2, CW]),
                                  ALU.mult).then_inc(z_done, 1)

            def low(m, k, s):
                c = 2 * m + k
                dve.wait_ge(high_done, STEPS * c + s + 1)
                if seen(m, k) >= 1:
                    dve.wait_ge(step_done, STEPS * (c - 1) + s + 1)
                dve.tensor_tensor(z_low[:, 2 * s, :], z[:, (k + s) % 2, 0:CW],
                                  z_high[:, 2 * s, :].bitcast(F32), ALU.subtract).then_inc(low_a_done, 1)

            def turned_to_low(m, k):
                dve.wait_ge(turned_high, 2 * m + k + 1)
                dve.tensor_tensor(x1t_low[:, :], turned[:, :], x1t_high[:, :].bitcast(F32), ALU.subtract)\
                    .then_inc(turned_low, 1)

            def p_to_low(m, k, g, acc=p_acc[:, 0:GW]):
                c = 2 * m + k
                dve.wait_ge(p_high_done, GROUPS * c + g + 1)
                dve.tensor_tensor(p_low[:, :, batch(c, g)], acc.rearrange("p (b j) -> p j b", b=GROUP),
                                  p_high[:, :, batch(c, g)].bitcast(F32), ALU.subtract)\
                    .then_inc(p_low_done, 1)

            def split_w1(part):
                dve.wait_ge(weights_high, 2 + part)
                at = slice(part * PJ, (part + 1) * PJ)
                dve.tensor_tensor(w1_low[:, at, :], stage[:, 0:PJ * H].rearrange("p (j n) -> p j n", n=H),
                                  w1_high[:, at, :].bitcast(F32), ALU.subtract).then_inc(weights_low, 1)

            def sum_x1(h):
                dve.wait_ge(p_low_done, GROUPS * CHUNKS // 2 * (h + 1))
                if h >= 1:
                    dve.wait_ge(stored, 2 * 16 * h)
                dve.tensor_tensor(sums[:, 0, :], p_high[:, F, :].bitcast(F32), p_low[:, F, :].bitcast(F32),
                                  ALU.add).then_inc(x1_sums, 1)

            def chunk(m, k):
                last, before = last_two(m, k)
                product(m, k, 0)
                if before:
                    p_to_low(*before, 1)
                product(m, k, 1)
                low(m, k, 0)
                if before:
                    p_to_low(*before, 2)
                product(m, k, 2)
                low(m, k, 1)
                if before:
                    p_to_low(*before, 3)
                low(m, k, 2)
                if last:
                    turned_to_low(*last)
                if middle(m, k):
                    sum_x1(0)
                if last:
                    p_to_low(*last, 0)

            dve.wait_ge(weights_in, 2 * 16)
            w0 = stage[:, 0:TILES * H]
            dve.tensor_tensor(w0, w0, stage[:, TILES * H:], ALU.add).then_inc(w0_summed, 1)
            dve.wait_ge(weights_high, 1)
            w0 = w0.rearrange("p (t n) -> p t n", n=H)
            dve.tensor_tensor(w0_low[:, :, :], w0[:, 0:FULL, :], w0_high[:, 0:FULL, :].bitcast(F32),
                              ALU.subtract).then_inc(weights_low, 1)
            for at in (SQUARE_ROWS[1], SQUARE_ROWS[3]):
                part = w0_high[at:at + 32, FULL, :]
                dve.tensor_tensor(part, w0[at:at + 32, FULL, :], part.bitcast(F32), ALU.subtract)\
                    .then_inc(weights_low, 1)
            chunk(0, 0)
            split_w1(0)
            chunk(0, 1)
            split_w1(1)
            with dve.Fori(1, MIDDLE) as m:
                chunk(m, 0)
                chunk(m, 1)
            split_w1(2)
            chunk(MIDDLE, 0)
            chunk(MIDDLE, 1)
            with dve.Fori(MIDDLE + 1, END) as m:
                chunk(m, 0)
                chunk(m, 1)
            chunk(END, 0)
            chunk(END, 1)
            for g in range(1, GROUPS):
                p_to_low(END, 0, g)
            turned_to_low(END, 1)
            for g in range(GROUPS):
                p_to_low(END, 1, g, acc=last_acc[g])
            sum_x1(1)

        @block.tensor
        def _(pe):
            def put_fields(m, k, s):
                c = 2 * m + k
                if s == 0:
                    pe.wait_ge(x_low_done, c + 1)
                if s == 0 and seen(m, k) >= 1:
                    pe.wait_ge(z_done, 3 * c)
                if s == 1 and seen(m, k) >= 1:
                    pe.wait_ge(high_done, STEPS * c)
                if s >= 2:
                    pe.wait_ge(z_done, 3 * c + s - 1)
                for n, t in enumerate(range(2 * s, min(2 * s + 2, TILES))):
                    mm = pe.matmul(placed[s % 2][:, n * CW:(n + 1) * CW], place[:, t, :], x_split[:, k, :],
                                   start=True, stop=True)
                mm.then_inc(placed_done, 1)

            def layer0(m, k, s):
                c = 2 * m + k
                if s == 0 and seen(m, k) >= 2:
                    pe.wait_ge(x1_out, c - 1)
                pe.wait_ge(low_b_done, STEPS * c + s + 1)
                acc = x1_acc[k][:, :]
                if s == STEPS - 1:
                    mm = pe.matmul(acc, w0_high[:, FULL, :], z_high[:, FULL, :], start=False, stop=True)
                else:
                    pe.wait_ge(low_a_done, 3 * c + s + 1)
                    for t in (2 * s, 2 * s + 1):
                        pe.matmul(acc, w0_high[:, t, :], z_high[:, t, :], start=(t == 0), stop=False)
                        pe.matmul(acc, w0_high[:, t, :], z_low[:, t, :], start=False, stop=False)
                        mm = pe.matmul(acc, w0_low[:, t, :], z_high[:, t, :], start=False, stop=False)
                mm.then_inc(step_done, 1)

            def turn_x1(m, k):
                c = 2 * m + k
                pe.wait_ge(x1_out, c + 1)
                if seen(m, k) >= 1:
                    pe.wait_ge(turned_low, c)
                for g in range(GROUPS):
                    at = slice(g * P, (g + 1) * P)
                    mm = pe.transpose(turned[:, at], x1[:, at], ident[:, :])
                mm.then_inc(x1_turned, 1)

            def group(m, k, g, acc=p_acc[:, 0:GW], last_bank=False):
                c = 2 * m + k
                if g == 0:
                    pe.wait_ge(turned_low, c + 1)
                if g % 2 == 0:
                    pe.wait_ge(blocks_loaded[g // 2], 16 * GROUP * (c + 1))
                if not last_bank and (g >= 1 or seen(m, k) >= 1):
                    pe.wait_ge(p_low_done, GROUPS * c + g)
                rows = slice(g * P, (g + 1) * P)
                x_high, x_low = (blocks[:, g // 2, n, g % 2, :] for n in range(2))
                pe.matmul(acc, x1t_high[:, rows], x_high, start=True, stop=False)
                pe.matmul(acc, x1t_high[:, rows], x_low, start=False, stop=False)
                pe.matmul(acc, x1t_low[:, rows], x_high, start=False, stop=True).then_inc(p_done, 1)

            def layer1(h):
                pe.wait_ge(p_low_done, GROUPS * CHUNKS // 2 * (h + 1))
                pe.wait_ge(weights_low, W1_DONE)
                for j in range(F):
                    pe.matmul(out_acc, w1_high[:, j, :], p_high[:, j, :], start=(j == 0), stop=False)
                    pe.matmul(out_acc, w1_high[:, j, :], p_low[:, j, :], start=False, stop=False)
                    mm = pe.matmul(out_acc, w1_low[:, j, :], p_high[:, j, :], start=False, stop=(j == F - 1))
                mm.then_inc(out_done, 1)

            def chunk(m, k, ahead=True):
                last, before = last_two(m, k)
                following = (m, 1) if k == 0 else (m + 1, 0)
                for s in range(STEPS):
                    layer0(m, k, s)
                    if s == 0:
                        put_fields(m, k, STEPS - 1)
                        if before:
                            group(*before, GROUPS - 1)
                        if last:
                            turn_x1(*last)
                        continue
                    if ahead:
                        put_fields(*following, s - 1)
                    if middle(m, k) and s == 1:
                        layer1(0)
                        pe.wait_ge(out_copied, 1)
                    if last:
                        group(*last, s - 1)

            pe.wait_ge(place_ready, 1)
            for s in range(STEPS - 1):
                put_fields(0, 0, s)
            pe.wait_ge(weights_low, W0_DONE)
            pe.wait_ge(constants_in[1], 16)
            chunk(0, 0)
            chunk(0, 1)
            with pe.Fori(1, MIDDLE) as m:
                chunk(m, 0)
                chunk(m, 1)
            chunk(MIDDLE, 0)
            chunk(MIDDLE, 1)
            with pe.Fori(MIDDLE + 1, END) as m:
                chunk(m, 0)
                chunk(m, 1)
            chunk(END, 0)
            chunk(END, 1, ahead=False)
            group(END, 0, GROUPS - 1)
            turn_x1(END, 1)
            for g in range(GROUPS):
                group(END, 1, g, acc=last_acc[g], last_bank=(g >= 1))
            layer1(1)


def kernel(r_x_emb, L0_rec_W0, L0_rec_W1):
    import concourse.bacc as bacc
    from concourse.bass_utils import run_bass_kernel_spmd

    x, w0, w1 = (np.asarray(a) for a in (r_x_emb, L0_rec_W0, L0_rec_W1))
    pairs, squares = plan_pairs()

    placing = np.zeros((P, TILES, P), np.float32)
    for p in range(P):
        for t in range(FULL):
            placing[[pairs[p][t][1], 64 + pairs[p][t][1]], t, p] = 1
    for at in SQUARE_ROWS:
        for n, i in enumerate(squares):
            placing[[i, 64 + i], FULL, at + n] = 1
    owner = np.repeat(np.eye(GROUP, dtype=np.float32), D, axis=0)

    w0 = w0.reshape(H, F, F)
    w0_ij, w0_ji = (np.zeros((P, TILES, H), np.float32) for _ in range(2))
    for p in range(P):
        for t, (i, j) in enumerate(pairs[p]):
            w0_ij[p, t] = w0[:, i, j]
            if i != j:
                w0_ji[p, t] = w0[:, j, i]
    for at in SQUARE_ROWS:
        for n, i in enumerate(squares):
            w0_ij[at + n, FULL] = w0[:, i, i]
    ins = {
        "x_rows": x.transpose(1, 0, 2).reshape(F, COLS)[ROW_FIELD],
        "x_groups": x.transpose(0, 2, 1).reshape(B // GROUP, P, F).transpose(1, 0, 2),
        "placing": placing.reshape(P, TILES * P),
        "identity": np.eye(P, dtype=np.float32),
        "owner": owner,
        "w0_ij": w0_ij.reshape(P, TILES * H),
        "w0_ji": w0_ji.reshape(P, TILES * H),
        "w1": w1.reshape(H, H, F).transpose(1, 2, 0),
    }
    ins = {name: np.ascontiguousarray(a) for name, a in ins.items()}
    nc = bacc.Bacc("TRN2", target_bir_lowering=False, num_devices=1)
    args = [nc.dram_tensor(name, a.shape, F32, kind="ExternalInput").ap() for name, a in ins.items()]
    out = nc.dram_tensor("out_t", (2 * H, B), F32, kind="ExternalOutput").ap()
    build(nc, *args, out)
    r = run_bass_kernel_spmd(nc, [ins], core_ids=[0])
    return np.ascontiguousarray(r.results[0]["out_t"].T)
```

```python
from contextlib import ExitStack

import concourse.bass as bass
import numpy as np
from concourse import mybir

F32 = mybir.dt.float32
F32R = mybir.dt.float32r
ALU = mybir.AluOpType
ACT = mybir.ActivationFunctionType

P = 128
B = 512
F = 39
D = 16
H = 128
COLS = B * D
CW = 512
CHUNKS = COLS // CW
GROUP = P // D
GROUPS = CW // P
FO = F + 1
GW = GROUP * FO
FULL = 6
TILES = FULL + 1
STEPS = TILES // 2 + 1
HALF = B // 2
PARTS = 3
PJ = F // PARTS
XS = 3

ROW_FIELD = (list(range(F)) + list(range(64 - F)) + list(range(F)) + list(range(64 - F, F)))
ROW_FIELD += list(range(P - len(ROW_FIELD)))
SQUARE_ROWS = (0, 32, 64, 96)


def plan_pairs():
    room = {i: FULL * ROW_FIELD.count(i) for i in range(F)}
    owned = {i: [] for i in range(F)}

    def place(pair, seen):
        for i in sorted(set(pair), key=lambda i: len(owned[i]) - room[i]):
            if i in seen:
                continue
            seen.add(i)
            if len(owned[i]) < room[i]:
                owned[i].append(pair)
                return True
            for other in list(owned[i]):
                if other[0] != other[1] and place(other, seen):
                    owned[i].remove(other)
                    owned[i].append(pair)
                    return True
        return False

    for i in range(F):
        for j in range(i + 1, F):
            assert place((i, j), set())
    squares = [i for i in range(F) if not place((i, i), set())]
    assert len(squares) == F * (F + 1) // 2 - FULL * P
    pairs = []
    for i in ROW_FIELD:
        pairs.append([(i, sum(pair) - i) for pair in (owned[i].pop() for _ in range(FULL))])
    return pairs, squares


def build(nc, x_rows, x_groups, placing, identity, owner, w0_ij, w0_ji, w1, out):
    ctx = ExitStack()
    with ctx:
        def sb(name, shape, dt=F32):
            return ctx.enter_context(nc.sbuf_tensor(name, shape, dt))

        def ps(name, shape):
            return ctx.enter_context(nc.psum_tensor(name, shape, F32))

        def sem(name):
            return ctx.enter_context(nc.semaphore(name))

        with nc.sbuf_tensor("landed", [P, (3 * TILES + F) * H], F32) as landed:
            placing_in = landed[:, 0:TILES * H].rearrange("p (t n) -> p t n", n=H)
            w0_in = landed[:, TILES * H:2 * TILES * H].rearrange("p (t n) -> p t n", n=H)
            w0_ji_in = landed[:, 2 * TILES * H:3 * TILES * H].rearrange("p (t n) -> p t n", n=H)
            w1_in = landed[:, 3 * TILES * H:].rearrange("p (j n) -> p j n", n=H)
        p_high = sb("p_high", [P, FO, HALF], F32R)
        p_low = sb("p_low", [P, FO, HALF], F32R)
        w0_high = sb("w0_high", [P, TILES, H], F32R)
        w0_low = sb("w0_low", [P, FULL, H], F32R)
        w1_high = sb("w1_high", [P, F, H], F32R)
        w1_low = sb("w1_low", [P, F, H], F32R)
        place = sb("place", [P, TILES, P], F32R)
        ident = sb("ident", [P, P])
        ones8 = sb("ones8", [P, GROUP])
        x_in = sb("x_in", [P, XS * CW])
        x_split = sb("x_split", [P, 2, CW], F32R)
        z = sb("z", [P, 2, 2 * CW])
        squares = sb("squares", [P, CW])
        z_high = sb("z_high", [P, TILES, CW], F32R)
        z_low = sb("z_low", [P, FULL, CW], F32R)
        x1 = sb("x1", [P, CW])
        x1t_high = sb("x1t_high", [P, CW], F32R)
        x1t_low = sb("x1t_low", [P, CW], F32R)
        xg_in = sb("xg_in", [P, 2, GROUPS, F])
        xg = sb("xg", [P, 2, 2, GROUPS, F], F32R)
        blocks = sb("blocks", [P, 2, 2, GROUPS, GW], F32R)
        sums = sb("sums", [P, 2, HALF])

        placed = [ps(f"placed{k}", [P, 2 * CW]) for k in range(2)]
        x1_acc = [ps(f"x1_acc{k}", [P, CW]) for k in range(2)]
        turned = x1_acc
        p_acc = [ps(f"p_acc{k}", [P, CW]) for k in range(2)]
        out_acc = p_acc[1][:, 0:HALF]

        constants_in = [sem(f"constants_in{k}") for k in range(3)]
        w0_loaded = sem("w0_loaded")
        w1_loaded = [sem(f"w1_loaded{n}") for n in range(PARTS)]
        weights_high = sem("weights_high")
        weights_low = sem("weights_low")
        w0_summed = sem("w0_summed")
        place_ready = sem("place_ready")
        blocks_zero = sem("blocks_zero")
        blocks_ones = sem("blocks_ones")
        x_loaded = [sem(f"x_loaded{k}") for k in range(2)]
        xg_loaded = [sem(f"xg_loaded{k}") for k in range(2)]
        x_high_done = sem("x_high_done")
        x_low_done = sem("x_low_done")
        xg_high_done = sem("xg_high_done")
        xg_low_done = sem("xg_low_done")
        blocks_loaded = [sem(f"blocks_loaded{k}") for k in range(2)]
        placed_done = sem("placed_done")
        z_done = sem("z_done")
        squares_done = sem("squares_done")
        high_done = sem("high_done")
        low_a_done = sem("low_a_done")
        low_b_done = sem("low_b_done")
        step_done = sem("step_done")
        x1_out = sem("x1_out")
        x1_turned = sem("x1_turned")
        turned_high = sem("turned_high")
        turned_low = sem("turned_low")
        p_done = sem("p_done")
        p_high_done = sem("p_high_done")
        p_low_done = sem("p_low_done")
        out_done = sem("out_done")
        out_copied = sem("out_copied")
        x1_sums = sem("x1_sums")
        stored = sem("stored")

        W0_DONE = 3
        W1_DONE = W0_DONE + PARTS
        MIDDLE, END = CHUNKS // 4, CHUNKS // 2 - 1
        block = ctx.enter_context(nc.Block())

        def slot(c):
            return bass.ds((c % XS) * CW, CW)

        def batch(c, g):
            return bass.ds((c % (CHUNKS // 2)) * (GROUPS * GROUP) + g * GROUP, GROUP)

        def seen(m, k):
            return min(2 * m + k, 2) if isinstance(m, int) else 2

        def middle(m, k):
            return isinstance(m, int) and (m, k) == (MIDDLE, 1)

        def last_two(m, k):
            last = ((m, 0) if k == 1 else (m - 1, 1)) if seen(m, k) >= 1 else None
            return last, (m - 1, k) if seen(m, k) >= 2 else None

        def following(m, k):
            return (m, 1) if k == 0 else (m + 1, 0)

        last_acc = [a[:, 0:GW] for a in (*p_acc, *placed)]

        @block.sync
        def _(sp):
            def load_x(c, k):
                sp.dma_start(x_in[:, slot(c)], x_rows[:, bass.ds(c * CW, CW)]).then_inc(x_loaded[k], 16)

            def load_xg(c, k):
                sp.dma_start(xg_in[:, k], x_groups[:, bass.ds(c * GROUPS, GROUPS), :])\
                    .then_inc(xg_loaded[k], 16)

            def chunk(m, k, load_ahead=True, load_g=True):
                c = 2 * m + k
                if load_ahead:
                    to, at = (c + XS) % XS * CW, (c + XS) * CW
                    if not isinstance(m, int):
                        to, at = sp.snap(to), sp.snap(at)
                    sp.wait_ge(x_low_done, c + 1)
                    sp.wait_ge(z_done, 3 * c + 3)
                    sp.wait_ge(x_loaded[1 - k], 16 * (m + 1 + k))
                    sp.dma_start(x_in[:, bass.ds(to, CW)], x_rows[:, bass.ds(at, CW)])\
                        .then_inc(x_loaded[1 - k], 16)
                sp.wait_ge(xg_high_done, c + 1)
                sp.wait_ge(xg_low_done, c + 1)
                if load_g:
                    load_xg(c + 2, k)
                if seen(m, k) == 0:
                    sp.wait_ge(blocks_ones, 1)
                if seen(m, k) >= 2:
                    sp.wait_ge(p_done, GROUPS * (c - 1))
                for b in range(GROUP):
                    rows = slice(D * b, D * b + D)
                    sp.dma_start(blocks[rows, k, :, :, FO * b:FO * b + F].bitcast(F32),
                                 xg[rows, k].bitcast(F32)).then_inc(blocks_loaded[k], 16)

            def store(h):
                sp.wait_ge(x1_sums, h + 1)
                sp.dma_start(out[0:H, h * HALF:(h + 1) * HALF], sums[:, 0, :]).then_inc(stored, 16)
                sp.wait_ge(out_copied, h + 1)
                sp.dma_start(out[H:2 * H, h * HALF:(h + 1) * HALF], sums[:, 1, :]).then_inc(stored, 16)

            load_x(0, 0)
            sp.dma_start(placing_in, placing[:, :, :]).then_inc(constants_in[0], 16)
            sp.dma_start(w0_in, w0_ij[:, :, :]).then_inc(w0_loaded, 16)
            sp.dma_start(w0_ji_in, w0_ji[:, :, :]).then_inc(w0_loaded, 16)
            load_x(1, 1)
            for k in range(2):
                load_xg(k, k)
            sp.dma_start(ones8[:, :], owner[:, :]).then_inc(constants_in[2], 16)
            sp.dma_start(ident[:, :], identity[:, :]).then_inc(constants_in[1], 16)
            sp.wait_ge(x_loaded[0], 16)
            load_x(2, 0)
            for n in range(PARTS):
                at = slice(n * PJ, (n + 1) * PJ)
                sp.dma_start(w1_in[:, at, :], w1[:, at, :]).then_inc(w1_loaded[n], 16)
            chunk(0, 0)
            chunk(0, 1)
            with sp.Fori(1, MIDDLE) as m:
                chunk(m, 0)
                chunk(m, 1)
            chunk(MIDDLE, 0)
            chunk(MIDDLE, 1)
            store(0)
            chunk(END - 2, 0)
            chunk(END - 2, 1)
            chunk(END - 1, 0)
            chunk(END - 1, 1, load_ahead=False)
            chunk(END, 0, load_ahead=False, load_g=False)
            chunk(END, 1, load_ahead=False, load_g=False)
            store(1)
            sp.wait_ge(stored, 4 * 16)

        @block.gpsimd
        def _(pool):
            def split_x(m, k):
                pool.wait_ge(x_high_done, 2 * m + k + 1)
                lower = x_split[64:P, k, :]
                pool.tensor_tensor(lower, x_in[64:P, slot(2 * m + k)], lower.bitcast(F32), ALU.subtract)\
                    .then_inc(x_low_done, 1)

            def split_xg(m, k):
                c = 2 * m + k
                pool.wait_ge(xg_high_done, c + 1)
                if seen(m, k) >= 2:
                    pool.wait_ge(blocks_loaded[k], 16 * GROUP * m)
                pool.tensor_tensor(xg[:, k, 1], xg_in[:, k], xg[:, k, 0].bitcast(F32), ALU.subtract)\
                    .then_inc(xg_low_done, 1)

            def low(m, k, s):
                c = 2 * m + k
                pool.wait_ge(high_done, STEPS * c + s + 1)
                if seen(m, k) >= 1:
                    pool.wait_ge(step_done, STEPS * (c - 1) + s + 1)
                pool.tensor_tensor(z_low[:, 2 * s + 1, :], z[:, (k + s) % 2, CW:2 * CW],
                                   z_high[:, 2 * s + 1, :].bitcast(F32), ALU.subtract)\
                    .then_inc(low_b_done, 1)

            def chunk(m, k, split_next=True, more=True):
                c = 2 * m + k
                pool.wait_ge(x_low_done, min(c + 2, CHUNKS) if isinstance(c, int) else c + 2)
                low(m, k, 1)
                split_xg(m, k)
                low(m, k, 2)
                pool.wait_ge(high_done, STEPS * c + STEPS)
                pool.wait_ge(low_b_done, STEPS * c + STEPS - 1)
                lower = z_high[64:P, TILES - 1, :]
                pool.tensor_tensor(lower, squares[64:P, :], lower.bitcast(F32), ALU.subtract)\
                    .then_inc(low_b_done, 1)
                if more:
                    pool.wait_ge(low_b_done, STEPS * c + STEPS)
                    low(*following(m, k), 0)
                if split_next:
                    pool.wait_ge(low_b_done, STEPS * c + STEPS + 1)
                    split_x(m + 1, k)

            pool.memset(blocks[:, :, :, :, :].bitcast(F32), 0.0).then_inc(blocks_zero, 1)
            low(0, 0, 0)
            pool.wait_ge(blocks_zero, 1)
            pool.wait_ge(low_b_done, 1)
            pool.wait_ge(x_low_done, 1)
            split_x(0, 1)
            chunk(0, 0)
            chunk(0, 1)
            with pool.Fori(1, END) as m:
                chunk(m, 0)
                chunk(m, 1)
            chunk(END, 0, split_next=False)
            chunk(END, 1, split_next=False, more=False)

        @block.scalar
        def _(act):
            def split_x(m, k):
                c = 2 * m + k
                act.wait_ge(x_loaded[k], 16 * (m + 1))
                if seen(m, k) >= 2:
                    act.wait_ge(placed_done, STEPS * (c - 1))
                act.activation(x_split[:, k, :], x_in[:, slot(c)], ACT.Copy).then_inc(x_high_done, 1)

            def split_xg(m, k):
                c = 2 * m + k
                act.wait_ge(xg_loaded[k], 16 * (m + 1))
                if seen(m, k) >= 2:
                    act.wait_ge(blocks_loaded[k], 16 * GROUP * m)
                act.activation(xg[:, k, 0], xg_in[:, k], ACT.Copy).then_inc(xg_high_done, 1)

            def high(m, k, s):
                c = 2 * m + k
                act.wait_ge(z_done, 3 * c + s + 1)
                if seen(m, k) >= 1:
                    act.wait_ge(step_done, STEPS * (c - 1) + s + 1)
                act.activation(z_high[:, 2 * s:2 * s + 2, :], z[:, (k + s) % 2, :], ACT.Copy)\
                    .then_inc(high_done, 1)

            def square(m, k):
                c = 2 * m + k
                act.wait_ge(placed_done, STEPS * (c + 1))
                if seen(m, k) >= 1:
                    act.wait_ge(step_done, STEPS * c)
                    act.wait_ge(low_b_done, STEPS * c)
                act.activation(squares[64:P, :], placed[1][64:P, 0:CW], ACT.Square).then_inc(squares_done, 1)
                act.wait_ge(squares_done, c + 1)
                act.activation(z_high[:, TILES - 1, :], placed[1][:, 0:CW], ACT.Square).then_inc(high_done, 1)

            def x1_to_sbuf(m, k):
                c = 2 * m + k
                act.wait_ge(step_done, STEPS * (c + 1))
                if seen(m, k) >= 1:
                    act.wait_ge(x1_turned, c)
                act.activation(x1[:, :], x1_acc[k][:, :], ACT.Copy).then_inc(x1_out, 1)

            def turned_to_high(m, k):
                c = 2 * m + k
                act.wait_ge(x1_turned, c + 1)
                if seen(m, k) >= 1:
                    act.wait_ge(p_done, GROUPS * c)
                act.activation(x1t_high[:, :], turned[k][:, :], ACT.Copy).then_inc(turned_high, 1)

            def p_to_high(m, k, g, acc=None):
                c = 2 * m + k
                acc = p_acc[g % 2][:, 0:GW] if acc is None else acc
                act.wait_ge(p_done, GROUPS * c + g + 1)
                act.activation(p_high[:, :, batch(c, g)], acc.rearrange("p (b j) -> p j b", b=GROUP),
                               ACT.Copy).then_inc(p_high_done, 1)

            def split_w1(part):
                act.wait_ge(w1_loaded[part], 16)
                at = slice(part * PJ, (part + 1) * PJ)
                act.activation(w1_high[:, at, :], w1_in[:, at, :], ACT.Copy).then_inc(weights_high, 1)

            def out_to_sbuf(h):
                act.wait_ge(out_done, h + 1)
                if h >= 1:
                    act.wait_ge(stored, 2 * 16 * h)
                act.activation(sums[:, 1, :], out_acc, ACT.Copy).then_inc(out_copied, 1)

            def chunk(m, k, split_next=True, more=True):
                last, before = last_two(m, k)
                then = following(m, k)
                split_xg(m, k)
                if before:
                    p_to_high(*before, 2)
                high(m, k, 2)
                if before:
                    p_to_high(*before, 3)
                if last:
                    turned_to_high(*last)
                square(m, k)
                if seen(m, k) < 2:
                    split_w1(2 * k)
                if middle(m, k):
                    high(*then, 0)
                    split_x(m + 1, k)
                    out_to_sbuf(0)
                    act.wait_ge(x1_sums, 1)
                    p_to_high(*last, 0)
                else:
                    if seen(m, k) == 1:
                        act.wait_ge(weights_low, W1_DONE)
                    if last:
                        p_to_high(*last, 0)
                    if more:
                        high(*then, 0)
                    if split_next:
                        split_x(m + 1, k)
                if last:
                    p_to_high(*last, 1)
                if more:
                    high(*then, 1)
                x1_to_sbuf(m, k)
                if seen(m, k) == 0:
                    split_w1(1)

            split_x(0, 0)
            act.wait_ge(w0_summed, 1)
            act.activation(w0_high[:, :, :], w0_in, ACT.Copy).then_inc(weights_high, 1)
            high(0, 0, 0)
            split_x(0, 1)
            high(0, 0, 1)
            act.wait_ge(constants_in[2], 16)
            act.wait_ge(blocks_zero, 1)
            act.activation(blocks[:, :, 0, :, F::FO],
                           ones8[:, :].unsqueeze(1).unsqueeze(1).to_broadcast([P, 2, GROUPS, GROUP]),
                           ACT.Copy).then_inc(blocks_ones, 1)
            chunk(0, 0)
            chunk(0, 1)
            with act.Fori(1, MIDDLE) as m:
                chunk(m, 0)
                chunk(m, 1)
            chunk(MIDDLE, 0)
            chunk(MIDDLE, 1)
            with act.Fori(MIDDLE + 1, END) as m:
                chunk(m, 0)
                chunk(m, 1)
            chunk(END, 0, split_next=False)
            chunk(END, 1, split_next=False, more=False)
            p_to_high(END, 0, 2)
            p_to_high(END, 0, 3)
            turned_to_high(END, 1)
            for g in range(GROUPS):
                p_to_high(END, 1, g, acc=last_acc[g])
            out_to_sbuf(1)

        @block.vector
        def _(dve):
            def product(m, k, s):
                c = 2 * m + k
                dve.wait_ge(placed_done, STEPS * c + s + 1)
                if s == 2:
                    dve.wait_ge(low_a_done, 3 * c + 1)
                    dve.wait_ge(low_b_done, STEPS * c + 1)
                elif seen(m, k) >= 1:
                    dve.wait_ge(low_a_done, 3 * (c - 1) + s + 2)
                    dve.wait_ge(low_b_done, STEPS * (c - 1) + s + 2)
                dve.tensor_tensor(z[:, (k + s) % 2, :].rearrange("p (t n) -> p t n", t=2),
                                  placed[s % 2][:, :].rearrange("p (t n) -> p t n", t=2),
                                  x_in[:, slot(c)].unsqueeze(1).to_broadcast([P, 2, CW]),
                                  ALU.mult).then_inc(z_done, 1)

            def low(m, k, s):
                c = 2 * m + k
                dve.wait_ge(high_done, STEPS * c + s + 1)
                if seen(m, k) >= 1:
                    dve.wait_ge(step_done, STEPS * (c - 1) + s + 1)
                dve.tensor_tensor(z_low[:, 2 * s, :], z[:, (k + s) % 2, 0:CW],
                                  z_high[:, 2 * s, :].bitcast(F32), ALU.subtract).then_inc(low_a_done, 1)

            def turned_to_low(m, k):
                dve.wait_ge(turned_high, 2 * m + k + 1)
                dve.tensor_tensor(x1t_low[:, :], turned[k][:, :], x1t_high[:, :].bitcast(F32), ALU.subtract)\
                    .then_inc(turned_low, 1)

            def p_to_low(m, k, g, acc=None):
                c = 2 * m + k
                acc = p_acc[g % 2][:, 0:GW] if acc is None else acc
                dve.wait_ge(p_high_done, GROUPS * c + g + 1)
                dve.tensor_tensor(p_low[:, :, batch(c, g)], acc.rearrange("p (b j) -> p j b", b=GROUP),
                                  p_high[:, :, batch(c, g)].bitcast(F32), ALU.subtract)\
                    .then_inc(p_low_done, 1)

            def split_w1(part):
                dve.wait_ge(weights_high, 2 + part)
                at = slice(part * PJ, (part + 1) * PJ)
                dve.tensor_tensor(w1_low[:, at, :], w1_in[:, at, :], w1_high[:, at, :].bitcast(F32),
                                  ALU.subtract).then_inc(weights_low, 1)

            def sum_x1(h):
                dve.wait_ge(p_low_done, GROUPS * CHUNKS // 2 * (h + 1))
                if h >= 1:
                    dve.wait_ge(stored, 2 * 16 * h)
                dve.tensor_tensor(sums[:, 0, :], p_high[:, F, :].bitcast(F32), p_low[:, F, :].bitcast(F32),
                                  ALU.add).then_inc(x1_sums, 1)

            def chunk(m, k, more=True):
                last, before = last_two(m, k)
                then = following(m, k)
                product(m, k, 2)
                low(m, k, 1)
                if before:
                    p_to_low(*before, 2)
                if before:
                    p_to_low(*before, 3)
                if last:
                    turned_to_low(*last)
                low(m, k, 2)
                if seen(m, k) < 2:
                    split_w1(2 * k)
                if more:
                    product(*then, 0)
                if middle(m, k):
                    sum_x1(0)
                if last:
                    p_to_low(*last, 0)
                if more:
                    product(*then, 1)
                    low(*then, 0)
                if last:
                    p_to_low(*last, 1)
                if seen(m, k) == 0:
                    split_w1(1)

            dve.wait_ge(constants_in[0], 16)
            dve.tensor_copy(place[:, :, :], placing_in).then_inc(place_ready, 1)
            dve.wait_ge(x_high_done, 1)
            lower = x_split[64:P, 0, :]
            dve.tensor_tensor(lower, x_in[64:P, 0:CW], lower.bitcast(F32), ALU.subtract).then_inc(x_low_done, 1)
            dve.wait_ge(w0_loaded, 2 * 16)
            dve.tensor_tensor(w0_in, w0_in, w0_ji_in, ALU.add).then_inc(w0_summed, 1)
            product(0, 0, 0)
            dve.wait_ge(weights_high, 1)
            dve.tensor_tensor(w0_low[:, :, :], w0_in[:, 0:FULL, :], w0_high[:, 0:FULL, :].bitcast(F32),
                              ALU.subtract).then_inc(weights_low, 1)
            for at in (SQUARE_ROWS[1], SQUARE_ROWS[3]):
                part = w0_high[at:at + 32, FULL, :]
                dve.tensor_tensor(part, w0_in[at:at + 32, FULL, :], part.bitcast(F32), ALU.subtract)\
                    .then_inc(weights_low, 1)
            low(0, 0, 0)
            product(0, 0, 1)
            chunk(0, 0)
            chunk(0, 1)
            with dve.Fori(1, MIDDLE) as m:
                chunk(m, 0)
                chunk(m, 1)
            chunk(MIDDLE, 0)
            chunk(MIDDLE, 1)
            with dve.Fori(MIDDLE + 1, END) as m:
                chunk(m, 0)
                chunk(m, 1)
            chunk(END, 0)
            chunk(END, 1, more=False)
            p_to_low(END, 0, 2)
            p_to_low(END, 0, 3)
            turned_to_low(END, 1)
            for g in range(GROUPS):
                p_to_low(END, 1, g, acc=last_acc[g])
            sum_x1(1)

        @block.tensor
        def _(pe):
            def put_fields(m, k, s):
                c = 2 * m + k
                if s == 0:
                    pe.wait_ge(x_low_done, c + 1)
                if s == 0 and seen(m, k) >= 1:
                    pe.wait_ge(z_done, 3 * c)
                if s == 1 and seen(m, k) >= 1:
                    pe.wait_ge(high_done, STEPS * c)
                if s >= 2:
                    pe.wait_ge(z_done, 3 * c + s - 1)
                for n, t in enumerate(range(2 * s, min(2 * s + 2, TILES))):
                    mm = pe.matmul(placed[s % 2][:, n * CW:(n + 1) * CW], place[:, t, :], x_split[:, k, :],
                                   start=True, stop=True)
                mm.then_inc(placed_done, 1)

            def layer0(m, k, s):
                c = 2 * m + k
                if s == 0 and seen(m, k) >= 2:
                    pe.wait_ge(turned_low, c - 1)
                pe.wait_ge(low_b_done, STEPS * c + s + 1)
                acc = x1_acc[k][:, :]
                if s == STEPS - 1:
                    mm = pe.matmul(acc, w0_high[:, FULL, :], z_high[:, FULL, :], start=False, stop=True)
                else:
                    pe.wait_ge(low_a_done, 3 * c + s + 1)
                    for t in (2 * s, 2 * s + 1):
                        pe.matmul(acc, w0_high[:, t, :], z_high[:, t, :], start=(t == 0), stop=False)
                        pe.matmul(acc, w0_high[:, t, :], z_low[:, t, :], start=False, stop=False)
                        mm = pe.matmul(acc, w0_low[:, t, :], z_high[:, t, :], start=False, stop=False)
                mm.then_inc(step_done, 1)

            def turn_x1(m, k):
                c = 2 * m + k
                pe.wait_ge(x1_out, c + 1)
                for g in range(GROUPS):
                    at = slice(g * P, (g + 1) * P)
                    mm = pe.transpose(turned[k][:, at], x1[:, at], ident[:, :])
                mm.then_inc(x1_turned, 1)

            def group(m, k, g, acc=None):
                c = 2 * m + k
                if g == 0:
                    pe.wait_ge(turned_low, c + 1)
                    pe.wait_ge(blocks_loaded[k], 16 * GROUP * (m + 1))
                if acc is None:
                    acc = p_acc[g % 2][:, 0:GW]
                    if g >= 2 or seen(m, k) >= 1:
                        pe.wait_ge(p_low_done, GROUPS * c + g - 1)
                rows = slice(g * P, (g + 1) * P)
                x_high, x_low = (blocks[:, k, n, g, :] for n in range(2))
                pe.matmul(acc, x1t_high[:, rows], x_high, start=True, stop=False)
                pe.matmul(acc, x1t_high[:, rows], x_low, start=False, stop=False)
                pe.matmul(acc, x1t_low[:, rows], x_high, start=False, stop=True).then_inc(p_done, 1)

            def layer1(h):
                pe.wait_ge(p_low_done, GROUPS * CHUNKS // 2 * (h + 1))
                pe.wait_ge(weights_low, W1_DONE)
                for j in range(F):
                    pe.matmul(out_acc, w1_high[:, j, :], p_high[:, j, :], start=(j == 0), stop=False)
                    pe.matmul(out_acc, w1_high[:, j, :], p_low[:, j, :], start=False, stop=False)
                    mm = pe.matmul(out_acc, w1_low[:, j, :], p_high[:, j, :], start=False, stop=(j == F - 1))
                mm.then_inc(out_done, 1)

            def chunk(m, k, ahead=True):
                last, before = last_two(m, k)
                for s in range(STEPS):
                    if s == 0:
                        put_fields(m, k, STEPS - 1)
                    elif ahead:
                        put_fields(*following(m, k), s - 1)
                    layer0(m, k, s)
                    if middle(m, k) and s == 1:
                        layer1(0)
                    if middle(m, k) and s == 2:
                        pe.wait_ge(out_copied, 1)
                    if s == 0 and before:
                        group(*before, GROUPS - 1)
                    if s == 0 and last:
                        turn_x1(*last)
                    if s >= 1 and last:
                        group(*last, s - 1)

            pe.wait_ge(place_ready, 1)
            for s in range(STEPS - 1):
                put_fields(0, 0, s)
            pe.wait_ge(weights_low, W0_DONE)
            pe.wait_ge(constants_in[1], 16)
            chunk(0, 0)
            chunk(0, 1)
            with pe.Fori(1, MIDDLE) as m:
                chunk(m, 0)
                chunk(m, 1)
            chunk(MIDDLE, 0)
            chunk(MIDDLE, 1)
            with pe.Fori(MIDDLE + 1, END) as m:
                chunk(m, 0)
                chunk(m, 1)
            chunk(END, 0)
            chunk(END, 1, ahead=False)
            group(END, 0, GROUPS - 1)
            turn_x1(END, 1)
            for g in range(GROUPS):
                if g < 2:
                    pe.wait_ge(p_low_done, GROUPS * (CHUNKS - 1) + g - 1)
                group(END, 1, g, acc=last_acc[g])
            layer1(1)


def kernel(r_x_emb, L0_rec_W0, L0_rec_W1):
    import concourse.bacc as bacc
    from concourse.bass_utils import run_bass_kernel_spmd

    x, w0, w1 = (np.asarray(a) for a in (r_x_emb, L0_rec_W0, L0_rec_W1))
    pairs, squares = plan_pairs()

    placing = np.zeros((P, TILES, P), np.float32)
    for p in range(P):
        for t in range(FULL):
            placing[[pairs[p][t][1], 64 + pairs[p][t][1]], t, p] = 1
    for at in SQUARE_ROWS:
        for n, i in enumerate(squares):
            placing[[i, 64 + i], FULL, at + n] = 1
    owner = np.repeat(np.eye(GROUP, dtype=np.float32), D, axis=0)

    w0 = w0.reshape(H, F, F)
    w0_ij, w0_ji = (np.zeros((P, TILES, H), np.float32) for _ in range(2))
    for p in range(P):
        for t, (i, j) in enumerate(pairs[p]):
            w0_ij[p, t] = w0[:, i, j]
            if i != j:
                w0_ji[p, t] = w0[:, j, i]
    for at in SQUARE_ROWS:
        for n, i in enumerate(squares):
            w0_ij[at + n, FULL] = w0[:, i, i]
    ins = {
        "x_rows": x.transpose(1, 0, 2).reshape(F, COLS)[ROW_FIELD],
        "x_groups": x.transpose(0, 2, 1).reshape(B // GROUP, P, F).transpose(1, 0, 2),
        "placing": placing,
        "identity": np.eye(P, dtype=np.float32),
        "owner": owner,
        "w0_ij": w0_ij,
        "w0_ji": w0_ji,
        "w1": w1.reshape(H, H, F).transpose(1, 2, 0),
    }
    ins = {name: np.ascontiguousarray(a) for name, a in ins.items()}
    nc = bacc.Bacc("TRN2", target_bir_lowering=False, num_devices=1)
    args = [nc.dram_tensor(name, a.shape, F32, kind="ExternalInput").ap() for name, a in ins.items()]
    out = nc.dram_tensor("out_t", (2 * H, B), F32, kind="ExternalOutput").ap()
    build(nc, *args, out)
    r = run_bass_kernel_spmd(nc, [ins], core_ids=[0])
    return np.ascontiguousarray(r.results[0]["out_t"].T)
```

```python
from contextlib import ExitStack

import concourse.bass as bass
import numpy as np
from concourse import mybir

F32 = mybir.dt.float32
F32R = mybir.dt.float32r
ALU = mybir.AluOpType
ACT = mybir.ActivationFunctionType

P = 128
B = 512
F = 39
D = 16
H = 128
COLS = B * D
CW = 512
CHUNKS = COLS // CW
GROUP = P // D
GROUPS = CW // P
FO = F + 1
GW = GROUP * FO
FULL = 6
TILES = FULL + 1
STEPS = TILES // 2 + 1
HALF = B // 2
SENT = 4
PUTS = 2
XW = (1 + SENT) * CW
W0_PARTS = (slice(0, 2), slice(2, 4), slice(4, TILES))
W1_PARTS = 3
WARM = 3
LATE = 30
PLAIN = F - LATE
LATE_W1 = 3
LF = 5
LATE_PARTS = 2 * LATE // LF
LATE_SLOTS = 6
XS = 3

ROW_FIELD = (list(range(F)) + list(range(64 - F)) + list(range(F)) + list(range(64 - F, F)))
ROW_FIELD += list(range(P - len(ROW_FIELD)))
SQUARE_ROWS = (0, 32, 64, 96)


def plan_pairs():
    room = {i: FULL * ROW_FIELD.count(i) for i in range(F)}
    owned = {i: [] for i in range(F)}

    def place(pair, seen):
        for i in sorted(set(pair), key=lambda i: len(owned[i]) - room[i]):
            if i in seen:
                continue
            seen.add(i)
            if len(owned[i]) < room[i]:
                owned[i].append(pair)
                return True
            for other in list(owned[i]):
                if other[0] != other[1] and place(other, seen):
                    owned[i].remove(other)
                    owned[i].append(pair)
                    return True
        return False

    for i in range(F):
        for j in range(i + 1, F):
            assert place((i, j), set())
    squares = [i for i in range(F) if not place((i, i), set())]
    assert len(squares) == F * (F + 1) // 2 - FULL * P
    pairs = []
    for i in ROW_FIELD:
        pairs.append([(i, sum(pair) - i) for pair in (owned[i].pop() for _ in range(FULL))])
    return pairs, squares


def build(nc, x_rows, x_groups, placing, identity, owner, w0, w1, out):
    ctx = ExitStack()
    with ctx:
        def sb(name, shape, dt=F32):
            return ctx.enter_context(nc.sbuf_tensor(name, shape, dt))

        def ps(name, shape):
            return ctx.enter_context(nc.psum_tensor(name, shape, F32))

        def sem(name):
            return ctx.enter_context(nc.semaphore(name))

        with nc.sbuf_tensor("landed", [P, FO * B], F32) as landed:
            w0_in = landed[:, 0:2 * TILES * H].rearrange("p (a t n) -> p a t n", a=2, n=H)
            place_in = landed[:, 2 * TILES * H:(3 * TILES - SENT) * H].rearrange("p (t n) -> p t n", n=H)
        with nc.sbuf_tensor("p_low", [P, FO, B], F32R) as p_low:
            pass
        p = sb("p", [P, FO, B])
        w0_high = sb("w0_high", [P, TILES, H], F32R)
        w0_low = sb("w0_low", [P, FULL, H], F32R)
        w1_in = sb("w1_in", [P, F * H])
        place = sb("place", [P, TILES - SENT, P], F32R)
        ident = sb("ident", [P, P])
        ones8 = sb("ones8", [P, GROUP])
        with nc.sbuf_tensor("late", [P, (2 * LATE + LATE_SLOTS * LF * HALF // H) * H], F32R) as late:
            w1_high, w1_low = (late[:, n * LATE * H:(n + 1) * LATE * H] for n in range(2))
            p_high = late[:, 2 * LATE * H:].rearrange("p (s j b) -> p s j b", s=LATE_SLOTS, j=LF)
        x_in = sb("x_in", [P, XS * XW])
        x_split = sb("x_split", [P, 2, CW], F32R)
        squares = sb("squares", [P, CW])
        z_high = sb("z_high", [P, TILES, CW], F32R)
        with nc.sbuf_tensor("z", [P, FULL, CW], F32) as z:
            pass
        z_low = sb("z_low", [P, FULL, CW], F32R)
        assert 2 * LATE * H + LATE_SLOTS * LF * HALF <= XS * XW + (2 + 1 + TILES + FULL) * CW
        x1 = sb("x1", [P, CW])
        x1t_high = sb("x1t_high", [P, CW], F32R)
        x1t_low = sb("x1t_low", [P, CW], F32R)
        xg_in = sb("xg_in", [P, 2, GROUPS, F])
        xg = sb("xg", [P, 2, 2, GROUPS, F], F32R)
        blocks = sb("blocks", [P, 2, 2, GROUPS, GW], F32R)
        x2_sum = sb("x2_sum", [P, B])

        placed = {2: ps("placed2", [P, 2 * CW]), 3: ps("placed3", [P, CW])}
        x1_acc = [ps(f"x1_acc{k}", [P, CW]) for k in range(2)]
        turned = x1_acc
        p_acc = [ps(f"p_acc{k}", [P, CW]) for k in range(2)]
        out_acc = [ps("out_acc0", [P, CW])[:, 0:HALF], x1_acc[1][:, 0:HALF]]
        last_turned = [x1_acc[0][:, 0:CW // 2], placed[2][:, 0:CW // 2]]
        last_acc = [a[:, 0:GW] for a in (*p_acc, placed[2][:, CW:], placed[3])]

        zeros_ready = sem("zeros_ready")
        place_loaded = sem("place_loaded")
        place_ready = sem("place_ready")
        ident_loaded = sem("ident_loaded")
        ones_loaded = sem("ones_loaded")
        w0_loaded = [sem(f"w0_loaded{n}") for n in range(3)]
        w1_loaded = sem("w1_loaded")
        w0_summed = sem("w0_summed")
        weights_high = sem("weights_high")
        weights_low = sem("weights_low")
        blocks_zero = sem("blocks_zero")
        blocks_ones = sem("blocks_ones")
        first_loaded = [sem(f"first_loaded{n}") for n in range(2)]
        x_loaded = [sem(f"x_loaded{k}") for k in range(2)]
        xg_loaded = [sem(f"xg_loaded{k}") for k in range(2)]
        x_high_done = sem("x_high_done")
        x_low_done = sem("x_low_done")
        xg_high_done = sem("xg_high_done")
        xg_low_done = sem("xg_low_done")
        blocks_loaded = [sem(f"blocks_loaded{k}") for k in range(2)]
        placed_done = sem("placed_done")
        z_done = sem("z_done")
        squares_done = sem("squares_done")
        high_done = sem("high_done")
        low_a_done = sem("low_a_done")
        low_b_done = sem("low_b_done")
        step_done = sem("step_done")
        x1_out = sem("x1_out")
        x1_turned = sem("x1_turned")
        turned_high = sem("turned_high")
        turned_low = sem("turned_low")
        p_done = sem("p_done")
        p_out = [sem(f"p_out{n}") for n in range(2)]
        w1_high_done = sem("w1_high_done")
        w1_low_done = sem("w1_low_done")
        p_high_done = sem("p_high_done")
        p_low_done = sem("p_low_done")
        late_done = sem("late_done")
        out_copied = sem("out_copied")
        stored = sem("stored")

        W0_DONE = 5
        END = CHUNKS // 2 - 1
        block = ctx.enter_context(nc.Block())

        def x_cols(c, first=0, n=1):
            return bass.ds((c % XS) * XW + first * CW, n * CW)

        def batch(c, g):
            return bass.ds(c * (GROUPS * GROUP) + g * GROUP, GROUP)

        def p_out_before(c, g):
            return c * (GROUPS // 2) + g // 2

        def late_w1(part):
            n = LATE // LATE_W1 * H
            return slice(part * n, (part + 1) * n), slice(PLAIN * H + part * n, PLAIN * H + (part + 1) * n)

        def late_p(part):
            h, n = divmod(part, LATE // LF)
            first = PLAIN + n * LF
            return slice(first, first + LF), slice(h * HALF, (h + 1) * HALF)

        def seen(m, k):
            return min(2 * m + k, 2) if isinstance(m, int) else 2

        def last_two(m, k):
            last = ((m, 0) if k == 1 else (m - 1, 1)) if seen(m, k) >= 1 else None
            return last, (m - 1, k) if seen(m, k) >= 2 else None

        def following(m, k):
            return (m, 1) if k == 0 else (m + 1, 0)

        @block.sync
        def _(sp):
            def chunk_of_x(at):
                return x_rows[bass.ds(at, P * XW)].rearrange("(p n) -> p n", n=XW)

            def load_x(c, k):
                sp.dma_start(x_in[:, x_cols(c, 0, 1 + SENT)], chunk_of_x(c * P * XW))\
                    .then_inc(x_loaded[k], 16)

            def load_xg(c, k):
                sp.dma_start(xg_in[:, k], x_groups[:, bass.ds(c * GROUPS, GROUPS), :])\
                    .then_inc(xg_loaded[k], 16)

            def fill_blocks(m, k, load_next):
                c = 2 * m + k
                sp.wait_ge(xg_high_done, c + 1)
                sp.wait_ge(xg_low_done, c + 1)
                if load_next:
                    load_xg(c + 2, k)
                if seen(m, k) == 0:
                    sp.wait_ge(blocks_ones, 1)
                if seen(m, k) >= 2:
                    sp.wait_ge(p_done, GROUPS * (c - 1))
                for b in range(GROUP):
                    rows = slice(D * b, D * b + D)
                    sp.dma_start(blocks[rows, k, :, :, FO * b:FO * b + F].bitcast(F32),
                                 xg[rows, k].bitcast(F32)).then_inc(blocks_loaded[k], 16)

            def chunk(m, k, load_ahead=True, load_next=True):
                c = 2 * m + k
                to, at = (c + XS) % XS * XW, (c + XS) * P * XW
                if not isinstance(m, int):
                    to, at = sp.snap(to), sp.snap(at)
                if load_ahead:
                    sp.wait_ge(z_done, 3 * c + 3)
                    sp.wait_ge(x_loaded[1 - k], 16 * (m + 1 + k))
                    sp.dma_start(x_in[:, bass.ds(to, XW)], chunk_of_x(at))\
                        .then_inc(x_loaded[1 - k], 16)
                fill_blocks(m, k, load_next)

            def load_w0(part):
                tiles = W0_PARTS[part]
                sp.dma_start(w0_in[:, :, tiles], w0[:, :, tiles]).then_inc(w0_loaded[part], 16)

            for n, (first, last) in enumerate(((0, 1), (1, 3))):
                at = slice(first * CW, last * CW)
                sp.dma_start(x_in[:, at], chunk_of_x(0)[:, at]).then_inc(first_loaded[n], 16)
            load_w0(0)
            at = slice(3 * CW, XW)
            sp.dma_start(x_in[:, at], chunk_of_x(0)[:, at]).then_inc(x_loaded[0], 16)
            sp.dma_start(place_in, placing[:, :, :]).then_inc(place_loaded, 16)
            load_w0(1)
            load_w0(2)
            load_xg(0, 0)
            sp.dma_start(ones8[:, :], owner[:, :]).then_inc(ones_loaded, 16)
            load_x(1, 1)
            load_xg(1, 1)
            sp.dma_start(ident[:, :], identity[:, :]).then_inc(ident_loaded, 16)
            sp.wait_ge(x_loaded[0], 16)
            load_x(2, 0)
            fill_blocks(0, 0, load_next=True)
            sp.wait_ge(z_done, 3)
            sp.wait_ge(x_loaded[1], 16)
            load_x(3, 1)
            chunk(0, 1)
            with sp.Fori(1, 1 + W1_PARTS) as m:
                chunk(m, 0)
                at = sp.snap((m - 1) * (F // W1_PARTS * H))
                sp.dma_start(w1_in[:, bass.ds(at, F // W1_PARTS * H)], w1[:, bass.ds(at, F // W1_PARTS * H)])\
                    .then_inc(w1_loaded, 16)
                chunk(m, 1)
            with sp.Fori(1 + W1_PARTS, END - 1) as m:
                chunk(m, 0)
                chunk(m, 1)
            chunk(END - 1, 0)
            chunk(END - 1, 1, load_ahead=False)
            chunk(END, 0, load_ahead=False, load_next=False)
            chunk(END, 1, load_ahead=False, load_next=False)
            for n in range(2):
                sp.wait_ge(p_out[n], GROUPS // 2 * CHUNKS)
            sp.dma_start(out[0:H, :], p[:, F, :]).then_inc(stored, 16)
            for h in range(2):
                sp.wait_ge(out_copied, h + 1)
                at = slice(h * HALF, (h + 1) * HALF)
                sp.dma_start(out[H:2 * H, at], x2_sum[:, at]).then_inc(stored, 16)
            sp.wait_ge(stored, 3 * 16)

        @block.gpsimd
        def _(pool):
            def split_x(m, k):
                pool.wait_ge(x_high_done, 2 * m + k + 1)
                lower = x_split[64:P, k, :]
                pool.tensor_tensor(lower, x_in[64:P, x_cols(2 * m + k)], lower.bitcast(F32), ALU.subtract)\
                    .then_inc(x_low_done, 1)

            def low(m, k, s):
                c = 2 * m + k
                pool.wait_ge(high_done, STEPS * c + s + 1)
                t = 2 * s + 1
                pool.tensor_tensor(z_low[:, t, :], z[:, t, :], z_high[:, t, :].bitcast(F32), ALU.subtract)\
                    .then_inc(low_b_done, 1)

            def low_squares(m, k):
                c = 2 * m + k
                pool.wait_ge(high_done, STEPS * c + STEPS)
                pool.wait_ge(low_b_done, STEPS * c + STEPS - 1)
                lower = z_high[64:P, TILES - 1, :]
                pool.tensor_tensor(lower, squares[64:P, :], lower.bitcast(F32), ALU.subtract)\
                    .then_inc(low_b_done, 1)
                pool.wait_ge(low_b_done, STEPS * c + STEPS)

            def chunk(m, k, split_next=True, more=True):
                c = 2 * m + k
                low(m, k, 2)
                low_squares(m, k)
                if more:
                    low(*following(m, k), 0)
                if split_next:
                    pool.wait_ge(low_b_done, STEPS * c + STEPS + 1)
                    split_x(m + 1, k)
                    pool.wait_ge(x_low_done, c + 3)
                if more:
                    low(*following(m, k), 1)

            pool.memset(blocks[:, :, :, :, :].bitcast(F32), 0.0).then_inc(blocks_zero, 1)
            for s in range(3):
                low(0, 0, s)
            low_squares(0, 0)
            low(0, 1, 0)
            pool.wait_ge(low_b_done, STEPS + 1)
            pool.wait_ge(x_low_done, 2)
            split_x(1, 0)
            pool.wait_ge(x_low_done, 3)
            low(0, 1, 1)
            chunk(0, 1)
            with pool.Fori(1, END) as m:
                chunk(m, 0)
                chunk(m, 1)
            chunk(END, 0, split_next=False)
            chunk(END, 1, split_next=False, more=False)
            for part in range(LATE_W1):
                pool.wait_ge(w1_high_done, part + 1)
                at, source = late_w1(part)
                pool.tensor_tensor(w1_low[:, at], w1_in[:, source], w1_high[:, at].bitcast(F32),
                                   ALU.subtract).then_inc(w1_low_done, 1)

        @block.scalar
        def _(act):
            def split_x(m, k):
                c = 2 * m + k
                if isinstance(c, int) and c == 0:
                    act.wait_ge(first_loaded[0], 16)
                else:
                    act.wait_ge(x_loaded[k], 16 * (m + 1))
                if seen(m, k) >= 2:
                    act.wait_ge(placed_done, PUTS * (c - 1))
                act.activation(x_split[:, k, :], x_in[:, x_cols(c)], ACT.Copy).then_inc(x_high_done, 1)

            def split_xg(m, k):
                c = 2 * m + k
                act.wait_ge(xg_loaded[k], 16 * (m + 1))
                if seen(m, k) >= 2:
                    act.wait_ge(blocks_loaded[k], 16 * GROUP * m)
                act.activation(xg[:, k, 0], xg_in[:, k], ACT.Copy).then_inc(xg_high_done, 1)

            def high(m, k, s):
                c = 2 * m + k
                act.wait_ge(z_done, 3 * c + s + 1)
                tiles = slice(2 * s, 2 * s + 2)
                act.activation(z_high[:, tiles, :], z[:, tiles, :], ACT.Copy)\
                    .then_inc(high_done, 1)

            def square(m, k):
                c = 2 * m + k
                act.wait_ge(placed_done, PUTS * c + 2)
                if seen(m, k) >= 1:
                    act.wait_ge(step_done, STEPS * c)
                    act.wait_ge(low_b_done, STEPS * c)
                act.activation(squares[64:P, :], placed[3][64:P, :], ACT.Square).then_inc(squares_done, 1)
                act.wait_ge(squares_done, c + 1)
                act.activation(z_high[:, TILES - 1, :], placed[3][:, :], ACT.Square).then_inc(high_done, 1)

            def x1_to_sbuf(m, k, pieces=1):
                c = 2 * m + k
                act.wait_ge(step_done, STEPS * (c + 1))
                if seen(m, k) >= 1:
                    act.wait_ge(x1_turned, c)
                for n in range(pieces):
                    at = slice(n * CW // pieces, (n + 1) * CW // pieces)
                    act.activation(x1[:, at], x1_acc[k][:, at], ACT.Copy).then_inc(x1_out, 1)

            def turned_to_high(m, k):
                c = 2 * m + k
                act.wait_ge(x1_turned, c + 1)
                if seen(m, k) >= 1:
                    act.wait_ge(p_done, GROUPS * c)
                act.activation(x1t_high[:, :], turned[k][:, :], ACT.Copy).then_inc(turned_high, 1)

            def last_turned_to_high(half):
                act.wait_ge(x1_turned, CHUNKS + half)
                if half == 0:
                    act.wait_ge(p_done, GROUPS * (CHUNKS - 1))
                at = slice(half * CW // 2, (half + 1) * CW // 2)
                act.activation(x1t_high[:, at], last_turned[half], ACT.Copy).then_inc(turned_high, 1)

            def p_to_sbuf(m, k, g, acc=None):
                c = 2 * m + k
                acc = p_acc[0][:, 0:GW] if acc is None else acc
                act.wait_ge(p_done, GROUPS * c + g + 1)
                act.activation(p[:, :, batch(c, g)], acc.rearrange("p (b j) -> p j b", b=GROUP),
                               ACT.Copy).then_inc(p_out[0], 1)

            def out_to_sbuf(h):
                act.wait_ge(late_done, (h + 1) * LATE // LF)
                act.activation(x2_sum[:, h * HALF:(h + 1) * HALF], out_acc[h], ACT.Copy).then_inc(out_copied, 1)

            def chunk(m, k, split_next=True, more=True):
                last, before = last_two(m, k)
                then = following(m, k)
                split_xg(m, k)
                if before:
                    p_to_sbuf(*before, 2)
                high(m, k, 2)
                if last:
                    turned_to_high(*last)
                square(m, k)
                if more:
                    high(*then, 0)
                if split_next:
                    split_x(m + 1, k)
                if seen(m, k) == 1:
                    act.wait_ge(weights_low, W0_DONE)
                if last:
                    p_to_sbuf(*last, 0)
                if more:
                    high(*then, 1)
                x1_to_sbuf(m, k, pieces=1 if more else 2)

            def late_w1_to_high(part):
                act.wait_ge(step_done, STEPS * CHUNKS)
                at, source = late_w1(part)
                act.activation(w1_high[:, at], w1_in[:, source], ACT.Copy).then_inc(w1_high_done, 1)

            def split_w0(part):
                tiles = W0_PARTS[part]
                act.wait_ge(w0_summed, part + 1)
                act.activation(w0_high[:, tiles, :], w0_in[:, 0, tiles], ACT.Copy).then_inc(weights_high, 1)

            split_x(0, 0)
            split_w0(0)
            high(0, 0, 0)
            act.wait_ge(place_loaded, 16)
            act.activation(place[:, :, :], place_in, ACT.Copy).then_inc(place_ready, 1)
            high(0, 0, 1)
            split_w0(1)
            act.wait_ge(ones_loaded, 16)
            act.wait_ge(blocks_zero, 1)
            act.activation(blocks[:, :, 0, :, F::FO],
                           ones8[:, :].unsqueeze(1).unsqueeze(1).to_broadcast([P, 2, GROUPS, GROUP]),
                           ACT.Copy).then_inc(blocks_ones, 1)
            split_xg(0, 0)
            high(0, 0, 2)
            split_w0(2)
            square(0, 0)
            split_x(0, 1)
            high(0, 1, 0)
            split_x(1, 0)
            high(0, 1, 1)
            x1_to_sbuf(0, 0)
            chunk(0, 1)
            with act.Fori(1, END) as m:
                chunk(m, 0)
                chunk(m, 1)
            chunk(END, 0, split_next=False)
            chunk(END, 1, split_next=False, more=False)
            p_to_sbuf(END, 0, 2)
            late_w1_to_high(0)
            for half in range(2):
                last_turned_to_high(half)
            late_w1_to_high(1)
            for g in (0, 2):
                p_to_sbuf(END, 1, g, acc=last_acc[g])
            late_w1_to_high(2)
            for n in range(2):
                act.wait_ge(p_out[n], GROUPS // 2 * CHUNKS)
            for part in range(LATE_PARTS):
                if part >= LATE_SLOTS:
                    act.wait_ge(late_done, part - LATE_SLOTS + 1)
                act.activation(p_high[:, part % LATE_SLOTS], p[:, *late_p(part)], ACT.Copy)\
                    .then_inc(p_high_done, 1)
            out_to_sbuf(0)
            out_to_sbuf(1)

        @block.vector
        def _(dve):
            def product(m, k, s):
                c = 2 * m + k
                if s == 2:
                    dve.wait_ge(placed_done, PUTS * c + 1)
                    second = placed[2][:, :]
                else:
                    if isinstance(c, int) and c == 0 and s == 0:
                        for part in first_loaded:
                            dve.wait_ge(part, 16)
                    else:
                        dve.wait_ge(x_loaded[k], 16 * (m + 1))
                    second = x_in[:, x_cols(c, 1 + 2 * s, 2)]
                if seen(m, k) >= 1:
                    dve.wait_ge(step_done, STEPS * (c - 1) + s + 1)
                dve.tensor_tensor(z[:, 2 * s:2 * s + 2, :],
                                  second.rearrange("p (t n) -> p t n", t=2),
                                  x_in[:, x_cols(c)].unsqueeze(1).to_broadcast([P, 2, CW]),
                                  ALU.mult).then_inc(z_done, 1)

            def low(m, k, s):
                dve.wait_ge(high_done, STEPS * (2 * m + k) + s + 1)
                t = 2 * s
                dve.tensor_tensor(z_low[:, t, :], z[:, t, :], z_high[:, t, :].bitcast(F32), ALU.subtract)\
                    .then_inc(low_a_done, 1)

            def split_xg(m, k):
                c = 2 * m + k
                dve.wait_ge(xg_high_done, c + 1)
                if seen(m, k) >= 2:
                    dve.wait_ge(blocks_loaded[k], 16 * GROUP * m)
                dve.tensor_tensor(xg[:, k, 1], xg_in[:, k], xg[:, k, 0].bitcast(F32), ALU.subtract)\
                    .then_inc(xg_low_done, 1)

            def turned_to_low(m, k):
                dve.wait_ge(turned_high, 2 * m + k + 1)
                dve.tensor_tensor(x1t_low[:, :], turned[k][:, :], x1t_high[:, :].bitcast(F32), ALU.subtract)\
                    .then_inc(turned_low, 1)

            def last_turned_to_low(half):
                dve.wait_ge(turned_high, CHUNKS + half)
                at = slice(half * CW // 2, (half + 1) * CW // 2)
                dve.tensor_tensor(x1t_low[:, at], last_turned[half], x1t_high[:, at].bitcast(F32),
                                  ALU.subtract).then_inc(turned_low, 1)

            def p_to_sbuf(m, k, g, acc=None):
                c = 2 * m + k
                acc = p_acc[1][:, 0:GW] if acc is None else acc
                dve.wait_ge(p_done, GROUPS * c + g + 1)
                dve.tensor_copy(p[:, :, batch(c, g)], acc.rearrange("p (b j) -> p j b", b=GROUP))\
                    .then_inc(p_out[1], 1)

            def chunk(m, k, more=True):
                last, before = last_two(m, k)
                then = following(m, k)
                low(m, k, 1)
                split_xg(m, k)
                if more:
                    product(*then, 0)
                if last:
                    turned_to_low(*last)
                low(m, k, 2)
                if before:
                    p_to_sbuf(*before, 3)
                if more:
                    product(*then, 1)
                    low(*then, 0)
                if seen(m, k) == 1:
                    dve.wait_ge(weights_low, W0_DONE)
                if last:
                    p_to_sbuf(*last, 1)
                if more:
                    product(*then, 2)

            def sum_w0(part):
                tiles = W0_PARTS[part]
                dve.wait_ge(w0_loaded[part], 16)
                dve.tensor_tensor(w0_in[:, 0, tiles], w0_in[:, 0, tiles], w0_in[:, 1, tiles], ALU.add)\
                    .then_inc(w0_summed, 1)

            def split_w0(part):
                at = W0_PARTS[part]
                tiles = slice(at.start, min(at.stop, FULL))
                dve.wait_ge(weights_high, part + 1)
                dve.tensor_tensor(w0_low[:, tiles, :], w0_in[:, 0, tiles], w0_high[:, tiles, :].bitcast(F32),
                                  ALU.subtract).then_inc(weights_low, 1)

            def split_low_squares():
                for at in (SQUARE_ROWS[1], SQUARE_ROWS[3]):
                    part = w0_high[at:at + 32, FULL, :]
                    dve.tensor_tensor(part, w0_in[at:at + 32, 0, FULL], part.bitcast(F32), ALU.subtract)\
                        .then_inc(weights_low, 1)

            def split_x(c):
                dve.wait_ge(x_high_done, c + 1)
                lower = x_split[64:P, c, :]
                dve.tensor_tensor(lower, x_in[64:P, x_cols(c)], lower.bitcast(F32), ALU.subtract)\
                    .then_inc(x_low_done, 1)

            dve.memset(x1[:, :], 0.0).then_inc(zeros_ready, 1)
            split_x(0)
            product(0, 0, 0)
            sum_w0(0)
            product(0, 0, 1)
            low(0, 0, 0)
            split_w0(0)
            sum_w0(1)
            low(0, 0, 1)
            split_w0(1)
            product(0, 0, 2)
            sum_w0(2)
            split_xg(0, 0)
            split_w0(2)
            product(0, 1, 0)
            low(0, 0, 2)
            split_low_squares()
            split_x(1)
            low(0, 1, 0)
            product(0, 1, 1)
            product(0, 1, 2)
            chunk(0, 1)
            with dve.Fori(1, END) as m:
                chunk(m, 0)
                chunk(m, 1)
            chunk(END, 0)
            chunk(END, 1, more=False)
            p_to_sbuf(END, 0, 3)
            for half in range(2):
                last_turned_to_low(half)
            for g in (1, 3):
                p_to_sbuf(END, 1, g, acc=last_acc[g])
            for part in range(LATE_PARTS):
                dve.wait_ge(p_high_done, part + 1)
                dve.tensor_tensor(p_low[:, *late_p(part)], p[:, *late_p(part)],
                                  p_high[:, part % LATE_SLOTS].bitcast(F32), ALU.subtract)\
                    .then_inc(p_low_done, 1)

        @block.tensor
        def _(pe):
            def put_fields(m, k, s):
                c = 2 * m + k
                if s == 2:
                    pe.wait_ge(x_low_done, c + 1)
                    if seen(m, k) >= 1:
                        pe.wait_ge(z_done, 3 * c)
                elif seen(m, k) >= 1:
                    pe.wait_ge(high_done, STEPS * c)
                for n, t in enumerate(range(2 * s, min(2 * s + 2, TILES))):
                    mm = pe.matmul(placed[s][:, n * CW:(n + 1) * CW], place[:, t - SENT, :],
                                   x_split[:, k, :], start=True, stop=True)
                mm.then_inc(placed_done, 1)

            def layer0(m, k, s):
                c = 2 * m + k
                if s == 0 and seen(m, k) >= 2:
                    pe.wait_ge(turned_low, c - 1)
                pe.wait_ge(low_b_done, STEPS * c + s + 1)
                acc = x1_acc[k][:, :]
                if seen(m, k) == 0:
                    pe.wait_ge(weights_low, s + 1 if s < 3 else W0_DONE)
                if s == STEPS - 1:
                    mm = pe.matmul(acc, w0_high[:, FULL, :], z_high[:, FULL, :], start=False, stop=True)
                else:
                    pe.wait_ge(low_a_done, 3 * c + s + 1)
                    for t in (2 * s, 2 * s + 1):
                        pe.matmul(acc, w0_high[:, t, :], z_high[:, t, :], start=(t == 0), stop=False)
                        pe.matmul(acc, w0_high[:, t, :], z_low[:, t, :], start=False, stop=False)
                        mm = pe.matmul(acc, w0_low[:, t, :], z_high[:, t, :], start=False, stop=False)
                mm.then_inc(step_done, 1)

            def turn_x1(m, k):
                if seen(m, k) == 0:
                    pe.wait_ge(ident_loaded, 16)
                pe.wait_ge(x1_out, 2 * m + k + 1)
                for g in range(GROUPS):
                    at = slice(g * P, (g + 1) * P)
                    mm = pe.transpose(turned[k][:, at], x1[:, at], ident[:, :])
                mm.then_inc(x1_turned, 1)

            def turn_last_x1():
                for half in range(2):
                    pe.wait_ge(x1_out, CHUNKS + half)
                    for g in range(GROUPS // 2):
                        at = (half * GROUPS // 2 + g) * P
                        mm = pe.transpose(last_turned[half][:, g * P:(g + 1) * P], x1[:, at:at + P],
                                          ident[:, :])
                    mm.then_inc(x1_turned, 1)

            def group(m, k, g, acc=None):
                c = 2 * m + k
                if g == 0:
                    pe.wait_ge(turned_low, c + 1)
                    pe.wait_ge(blocks_loaded[k], 16 * GROUP * (m + 1))
                if acc is None:
                    acc = p_acc[g % 2][:, 0:GW]
                    if g >= 2 or seen(m, k) >= 1:
                        pe.wait_ge(p_out[g % 2], p_out_before(c, g))
                rows = slice(g * P, (g + 1) * P)
                x_high, x_low = (blocks[:, k, n, g, :] for n in range(2))
                pe.matmul(acc, x1t_high[:, rows], x_high, start=True, stop=False)
                pe.matmul(acc, x1t_high[:, rows], x_low, start=False, stop=False)
                pe.matmul(acc, x1t_low[:, rows], x_high, start=False, stop=True).then_inc(p_done, 1)

            def layer1(h, fields):
                if fields.start == 0:
                    pe.wait_ge(w1_loaded, 16 * W1_PARTS)
                    for n in range(2):
                        pe.wait_ge(p_out[n], GROUPS // 2 * CHUNKS // 2 * (h + 1))
                for j in fields:
                    pe.matmul(out_acc[h], w1_in[:, j * H:(j + 1) * H], p[:, j, h * HALF:(h + 1) * HALF],
                              start=(j == 0), stop=False)

            def layer1_late():
                for part in range(LATE_PARTS):
                    pe.wait_ge(w1_low_done, min(part * LF * LATE_W1 // LATE + 1, LATE_W1))
                    pe.wait_ge(p_low_done, part + 1)
                    (fields, rows), h = late_p(part), part // (LATE // LF)
                    for n, j in enumerate(range(fields.start, fields.stop)):
                        at = slice((j - PLAIN) * H, (j - PLAIN + 1) * H)
                        high, low = p_high[:, part % LATE_SLOTS, n, :], p_low[:, j, rows]
                        pe.matmul(out_acc[h], w1_high[:, at], high, start=False, stop=False)
                        pe.matmul(out_acc[h], w1_high[:, at], low, start=False, stop=False)
                        mm = pe.matmul(out_acc[h], w1_low[:, at], high, start=False, stop=(j == F - 1))
                    mm.then_inc(late_done, 1)

            def chunk(m, k, ahead=True, fields=None):
                last, before = last_two(m, k)
                for s in range(STEPS):
                    if s in (1, 2) and ahead and seen(m, k) >= 1:
                        put_fields(*following(m, k), s + 1)
                    layer0(m, k, s)
                    if s == 0 and seen(m, k) == 1:
                        put_fields(m, k, 2)
                        put_fields(m, k, 3)
                    if s == 0 and before:
                        group(*before, GROUPS - 1)
                    if s == 0 and last:
                        turn_x1(*last)
                    if s == 1 and fields:
                        layer1(0, fields)
                    if s >= 1 and last:
                        group(*last, s - 1)

            pe.wait_ge(zeros_ready, 1)
            for n in range(WARM):
                pe.matmul(p_acc[0][:, :], x1[:, 0:P], x1[:, :], start=True, stop=True)
            pe.wait_ge(place_ready, 1)
            for s in (2, 3):
                put_fields(0, 0, s)
            chunk(0, 0)
            chunk(0, 1)
            with pe.Fori(1, END) as m:
                chunk(m, 0)
                chunk(m, 1)
            chunk(END, 0, fields=range(0, 1))
            chunk(END, 1, ahead=False, fields=range(1, 2))
            layer1(0, range(2, 3))
            group(END, 0, GROUPS - 1)
            layer1(0, range(3, 4))
            turn_last_x1()
            layer1(0, range(4, PLAIN - 2))
            for g in range(GROUPS):
                pe.wait_ge(turned_low, CHUNKS + g // 2)
                if g < 2:
                    pe.wait_ge(p_out[g], p_out_before(CHUNKS - 1, g))
                group(END, 1, g, acc=last_acc[g])
            layer1(0, range(PLAIN - 2, PLAIN))
            layer1(1, range(PLAIN))
            layer1_late()


def kernel(r_x_emb, L0_rec_W0, L0_rec_W1):
    import concourse.bacc as bacc
    from concourse.bass_utils import run_bass_kernel_spmd

    x, w0, w1 = (np.asarray(a) for a in (r_x_emb, L0_rec_W0, L0_rec_W1))
    pairs, squares = plan_pairs()

    placing = np.zeros((P, TILES - SENT, P), np.float32)
    for p in range(P):
        for t in range(SENT, FULL):
            placing[[pairs[p][t][1], 64 + pairs[p][t][1]], t - SENT, p] = 1
    for at in SQUARE_ROWS:
        for n, i in enumerate(squares):
            placing[[i, 64 + i], FULL - SENT, at + n] = 1
    owner = np.repeat(np.eye(GROUP, dtype=np.float32), D, axis=0)

    w0 = w0.reshape(H, F, F)
    w0_pairs = np.zeros((P, 2, TILES, H), np.float32)
    for p in range(P):
        for t, (i, j) in enumerate(pairs[p]):
            w0_pairs[p, 0, t] = w0[:, i, j]
            if i != j:
                w0_pairs[p, 1, t] = w0[:, j, i]
    for at in SQUARE_ROWS:
        for n, i in enumerate(squares):
            w0_pairs[at + n, 0, FULL] = w0[:, i, i]
    x_fields = x.transpose(1, 0, 2).reshape(F, COLS)
    sources = [ROW_FIELD] + [[pairs[p][t][1] for p in range(P)] for t in range(SENT)]
    ins = {
        "x_rows": x_fields[sources].reshape(1 + SENT, P, CHUNKS, CW).transpose(2, 1, 0, 3)
                                   .reshape(CHUNKS * P * XW),
        "x_groups": x.transpose(0, 2, 1).reshape(B // GROUP, P, F).transpose(1, 0, 2),
        "placing": placing,
        "identity": np.eye(P, dtype=np.float32),
        "owner": owner,
        "w0": w0_pairs,
        "w1": w1.reshape(H, H, F).transpose(1, 2, 0).reshape(H, F * H),
    }
    ins = {name: np.ascontiguousarray(a) for name, a in ins.items()}
    nc = bacc.Bacc("TRN2", target_bir_lowering=False, num_devices=1)
    args = [nc.dram_tensor(name, a.shape, F32, kind="ExternalInput").ap() for name, a in ins.items()]
    out = nc.dram_tensor("out_t", (2 * H, B), F32, kind="ExternalOutput").ap()
    build(nc, *args, out)
    r = run_bass_kernel_spmd(nc, [ins], core_ids=[0])
    return np.ascontiguousarray(r.results[0]["out_t"].T)
```
